# Optimizing a Trainium2 kernel written in Bass

```python
import numpy as np
import jax
import jax.numpy as jnp

def _softmax(x, axis=-1):
    return jax.nn.softmax(x, axis=axis)

def _gelu(x):
    return jax.nn.gelu(x, approximate=True)

def _silu(x):
    return jax.nn.silu(x)

def _sigmoid(x):
    return jax.nn.sigmoid(x)

def _layernorm(x, axis=-1, eps=1e-05):
    m = jnp.mean(x, axis=axis, keepdims=True)
    v = jnp.var(x, axis=axis, keepdims=True)
    return (x - m) / jnp.sqrt(v + eps)

def _scatter_add(tgt, idx, src, axis=0):
    return tgt.at[idx].add(src)

def _segment_sum(src, seg, n):
    return jax.ops.segment_sum(src, seg, n)
kernel_name = 'mk_gnn_resnorm_d2_gnn_r8_3acd85'

def setup_inputs(seed: int=0):
    np.random.seed(seed)
    _w = jnp.asarray

    def _rec_inputs():
        import jax
        import jax.numpy as jnp
        _gk = jax.random.key(seed)
        x = -0.0005121 + 1.001 * jax.random.normal(jax.random.fold_in(_gk, 1), (12500, 32), jnp.float32)
        src = jax.random.randint(jax.random.fold_in(_gk, 2), (400000,), 0, 12500, jnp.int32)
        dst = jnp.minimum((12500 * jax.random.uniform(jax.random.fold_in(_gk, 3), (400000,)) ** 2.0).astype(jnp.int32), 99999)
        _o = jnp.argsort(dst, stable=True)
        src = src[_o]
        dst = dst[_o]
        edge_attr_32 = 0.000196303 + 1.00016 * jax.random.normal(jax.random.fold_in(_gk, 11), (400000, 32), jnp.float32)
        return (x, src, dst, edge_attr_32)
    x, src, dst, edge_attr_32 = _rec_inputs()

    def _L0_gnn_setup():
        import jax, jax.numpy as jnp
        import numpy as np
        N_NODES = 12500
        N_EDGES = 400000
        D = 32

        def _gat(x, edge_index, W, att_s, att_d, bias, heads, ch, neg_slope):
            n = x.shape[0]
            h = (x @ W.T).reshape(n, heads, ch)
            a_s = (h * att_s[None]).sum(-1)
            a_d = (h * att_d[None]).sum(-1)
            src, dst = (edge_index[0], edge_index[1])
            logits = jax.nn.leaky_relu(a_s[src] + a_d[dst], neg_slope)
            m = jax.ops.segment_max(logits, dst, num_segments=n)
            m = jnp.where(jnp.isfinite(m), m, 0.0)
            ex = jnp.exp(logits - m[dst])
            denom = jax.ops.segment_sum(ex, dst, num_segments=n)
            alpha = ex / (denom[dst] + 1e-16)
            out = jax.ops.segment_sum(alpha[:, :, None] * h[src], dst, num_segments=n)
            return out.reshape(n, heads * ch) + bias
        key = jax.random.key(seed)
        ks = jax.random.split(key, 16)
        x = jax.random.normal(ks[0], (N_NODES, D), dtype=jnp.float32)
        edge_index = jax.random.randint(ks[1], (2, N_EDGES), 0, N_NODES, dtype=jnp.int64)
        s = 1.0 / np.sqrt(D)
        return {'x': x, 'edge_index': edge_index, 'W1': jax.random.normal(ks[2], (32, D), dtype=jnp.float32) * s, 'att_s1': jax.random.normal(ks[3], (2, 16), dtype=jnp.float32) * 0.05, 'att_d1': jax.random.normal(ks[4], (2, 16), dtype=jnp.float32) * 0.05, 'b1': jnp.full((32,), 0.1, dtype=jnp.float32), 'ea1': jnp.ones((1,), dtype=jnp.float32), 'W2': jax.random.normal(ks[5], (32, 32), dtype=jnp.float32) * s, 'att_s2': jax.random.normal(ks[6], (2, 16), dtype=jnp.float32) * 0.05, 'att_d2': jax.random.normal(ks[7], (2, 16), dtype=jnp.float32) * 0.05, 'b2': jnp.full((32,), 0.1, dtype=jnp.float32), 'W3': jax.random.normal(ks[8], (32, 32), dtype=jnp.float32) * s, 'att_s3': jax.random.normal(ks[9], (1, 32), dtype=jnp.float32) * 0.05, 'att_d3': jax.random.normal(ks[10], (1, 32), dtype=jnp.float32) * 0.05, 'b3': jnp.full((32,), 0.1, dtype=jnp.float32)}
    _L0_gnn_all = _L0_gnn_setup()
    _L0_gnn_in = {k: v for k, v in _L0_gnn_all.items() if k in ('W1', 'att_s1', 'att_d1', 'b1', 'ea1', 'W2', 'att_s2', 'att_d2', 'b2', 'W3', 'att_s3', 'att_d3', 'b3')}
    del _L0_gnn_all

    def _L1_gnn_setup():
        import jax, jax.numpy as jnp
        import numpy as np
        N_NODES = 6250
        N_EDGES = 100000
        X_DIM = 32
        E_DIM = 32
        HID = 64
        OUT = 32
        key = jax.random.key(seed)
        ks = jax.random.split(key, 6)
        x = jax.random.normal(ks[0], (N_NODES, X_DIM), dtype=jnp.float32)
        edge_index = jax.random.randint(ks[1], (2, N_EDGES), 0, N_NODES, dtype=jnp.int64)
        edge_attr = jax.random.normal(ks[2], (N_EDGES, E_DIM), dtype=jnp.float32)
        in_dim = 2 * X_DIM + E_DIM
        W1 = jax.random.normal(ks[3], (in_dim, HID), dtype=jnp.float32) * (1.0 / np.sqrt(in_dim))
        b1 = jnp.zeros((HID,), dtype=jnp.float32)
        W2 = jax.random.normal(ks[4], (HID, OUT), dtype=jnp.float32) * (1.0 / np.sqrt(HID))
        b2 = jnp.zeros((OUT,), dtype=jnp.float32)
        return {'x': x, 'edge_index': edge_index, 'edge_attr': edge_attr, 'W1': W1, 'b1': b1, 'W2': W2, 'b2': b2}
    _L1_gnn_all = _L1_gnn_setup()
    _L1_gnn_in = {k: v for k, v in _L1_gnn_all.items() if k in ('W1', 'b1', 'W2', 'b2')}
    del _L1_gnn_all
    return {'x': x, 'src': src, 'dst': dst, 'edge_attr_32': edge_attr_32, 'L0_gnn_W1': _L0_gnn_in['W1'], 'L0_gnn_att_s1': _L0_gnn_in['att_s1'], 'L0_gnn_att_d1': _L0_gnn_in['att_d1'], 'L0_gnn_b1': _L0_gnn_in['b1'], 'L0_gnn_ea1': _L0_gnn_in['ea1'], 'L0_gnn_W2': _L0_gnn_in['W2'], 'L0_gnn_att_s2': _L0_gnn_in['att_s2'], 'L0_gnn_att_d2': _L0_gnn_in['att_d2'], 'L0_gnn_b2': _L0_gnn_in['b2'], 'L0_gnn_W3': _L0_gnn_in['W3'], 'L0_gnn_att_s3': _L0_gnn_in['att_s3'], 'L0_gnn_att_d3': _L0_gnn_in['att_d3'], 'L0_gnn_b3': _L0_gnn_in['b3'], 'L1_gnn_W1': _L1_gnn_in['W1'], 'L1_gnn_b1': _L1_gnn_in['b1'], 'L1_gnn_W2': _L1_gnn_in['W2'], 'L1_gnn_b2': _L1_gnn_in['b2']}

def reference(x, src, dst, edge_attr_32, L0_gnn_W1, L0_gnn_att_s1, L0_gnn_att_d1, L0_gnn_b1, L0_gnn_ea1, L0_gnn_W2, L0_gnn_att_s2, L0_gnn_att_d2, L0_gnn_b2, L0_gnn_W3, L0_gnn_att_s3, L0_gnn_att_d3, L0_gnn_b3, L1_gnn_W1, L1_gnn_b1, L1_gnn_W2, L1_gnn_b2):
    import jax
    import jax.numpy as jnp

    def _L0_gnn_ref(x, edge_index, W1, att_s1, att_d1, b1, ea1, W2, att_s2, att_d2, b2, W3, att_s3, att_d3, b3):
        import jax, jax.numpy as jnp
        import numpy as np
        N_NODES = 12500
        N_EDGES = 400000
        D = 32

        def _gat(x, edge_index, W, att_s, att_d, bias, heads, ch, neg_slope):
            n = x.shape[0]
            h = (x @ W.T).reshape(n, heads, ch)
            a_s = (h * att_s[None]).sum(-1)
            a_d = (h * att_d[None]).sum(-1)
            src, dst = (edge_index[0], edge_index[1])
            logits = jax.nn.leaky_relu(a_s[src] + a_d[dst], neg_slope)
            m = jax.ops.segment_max(logits, dst, num_segments=n)
            m = jnp.where(jnp.isfinite(m), m, 0.0)
            ex = jnp.exp(logits - m[dst])
            denom = jax.ops.segment_sum(ex, dst, num_segments=n)
            alpha = ex / (denom[dst] + 1e-16)
            out = jax.ops.segment_sum(alpha[:, :, None] * h[src], dst, num_segments=n)
            return out.reshape(n, heads * ch) + bias
        h = _gat(x, edge_index, W1, att_s1, att_d1, b1, heads=2, ch=16, neg_slope=0.01)
        scale = jnp.tanh(ea1)[0]
        scale = jnp.where(scale < 0.1, 1.0, scale)
        h = h * scale
        h = h + 0.05 * jax.lax.stop_gradient(h)
        h = jax.nn.elu(h)
        h = jnp.clip(h, -3.0, 3.0)
        h = _gat(h, edge_index, W2, att_s2, att_d2, b2, heads=2, ch=16, neg_slope=0.2)
        h = jax.nn.elu(h)
        h = jnp.clip(h, -3.0, 3.0)
        out = _gat(h, edge_index, W3, att_s3, att_d3, b3, heads=1, ch=32, neg_slope=0.2)
        return out

    def _L1_gnn_ref(x, edge_index, edge_attr, W1, b1, W2, b2):
        import jax, jax.numpy as jnp
        import numpy as np
        N_NODES = 6250
        N_EDGES = 100000
        X_DIM = 32
        E_DIM = 32
        HID = 64
        OUT = 32
        num_nodes = x.shape[0]
        rol, col = (edge_index[0], edge_index[1])
        e_feat = jnp.concatenate([x[rol], x[col], edge_attr], axis=-1)
        h = jax.nn.relu(e_feat @ W1 + b1)
        v = h @ W2 + b2
        x_cand = jax.ops.segment_max(v, col, num_segments=num_nodes)
        return jnp.maximum(x_cand, x[:, -v.shape[-1]:])
    edge_index = jnp.stack([src, dst])
    x = _layernorm(x + _L0_gnn_ref(x, edge_index, L0_gnn_W1, L0_gnn_att_s1, L0_gnn_att_d1, L0_gnn_b1, L0_gnn_ea1, L0_gnn_W2, L0_gnn_att_s2, L0_gnn_att_d2, L0_gnn_b2, L0_gnn_W3, L0_gnn_att_s3, L0_gnn_att_d3, L0_gnn_b3), axis=-1)
    x = _layernorm(x + _L1_gnn_ref(x, edge_index, edge_attr_32, L1_gnn_W1, L1_gnn_b1, L1_gnn_W2, L1_gnn_b2), axis=-1)
    return x

_drawn_inputs = setup_inputs


def setup_inputs(seed=0):
    import zlib

    import numpy as np

    out = dict(_drawn_inputs(seed))
    spreads = {'L0_gnn_b1': (0.10000000149011612, 0.6),
     'L0_gnn_b2': (0.10000000149011612, 0.6),
     'L0_gnn_b3': (0.10000000149011612, 0.6),
     'L1_gnn_b1': (0.0, 0.1),
     'L1_gnn_b2': (0.0, 0.1)}
    factors = {'L0_gnn_att_d1': 64.0,
     'L0_gnn_att_s2': 31.169,
     'L0_gnn_att_d2': 64.0,
     'L0_gnn_att_s3': 64.0,
     'L0_gnn_att_d3': 64.0}
    for name, (base, spread) in spreads.items():
        noise = np.random.default_rng([zlib.crc32(name.encode()), seed]).standard_normal(out[name].shape)
        drawn = base * np.exp(spread * noise) if base else spread * noise
        out[name] = jnp.asarray(drawn.astype(out[name].dtype))
    for name, factor in factors.items():
        out[name] = (out[name] * factor).astype(out[name].dtype)
    return out
```

```python
import concourse.bass as bass
from concourse import mybir
from contextlib import ExitStack

N_NODES, N_EDGES, F = 12500, 400000, 32
HID = 64
P = 128
NT = 98
NP = P * NT
NQ = 4
L = 512
J = L // P
NC = 196
Q = NC * L
EP = NQ * Q
EL = EP + NP
ROW = F + 2
OW = F + 4
BIG = float(2 ** 126)
TU = 7
NU = NT // TU
LEAD = L
SAMPLES = EP // L
LAST_P = (N_NODES - (P - 1) * NT)
LN_EPS = 1e-5
HALF = NC // 2
assert (NQ - 1) * Q + (NC - 2) * L >= N_EDGES


def need(eng, sem, value):
    if isinstance(value, int) and value <= 0:
        return
    eng.wait_ge(sem, value)


def build(nc, I, out):
    fp32, bf16, i32 = mybir.dt.float32, mybir.dt.bfloat16, mybir.dt.int32
    ALU, ACT, AX = mybir.AluOpType, mybir.ActivationFunctionType, mybir.AxisListType
    ctx = ExitStack()
    with ctx:
        ctx.enter_context(nc.allow_non_contiguous_dma(reason="small parameter and index loads"))

        def dram(name, shape, dt):
            return nc.dram_tensor(name, shape, dt, kind="Internal").ap()

        def sb(name, shape, dt=fp32):
            return ctx.enter_context(nc.sbuf_tensor(name, shape, dt))

        def sem(name):
            return ctx.enter_context(nc.semaphore(name))

        def view(t, offset, dims, parts=P, p0=0):
            row = 1
            for n in t.shape[1:]:
                row *= n
            return bass.AP(tensor=t, offset=offset + p0 * row, ap=[[row, parts]] + dims)

        dstp = dram("dstp", (LEAD + EP,), i32)
        srcp = dram("srcp", (EP,), i32)
        rrow = dram("rrow", (EP,), bf16)
        startd = dram("startd", (NP + P,), fp32)
        table = dram("table", (NP, F), fp32)
        adtable = dram("adtable", (NP, 2), fp32)
        aux = dram("aux", (EL, 2), fp32)
        auxx = dram("auxx", (EL, F), fp32)
        state = dram("state", (EP, OW), fp32)
        vmax = dram("vmax", (EP, F), fp32)

        ident = sb("ident", [P, P])
        ones = sb("ones", [P, P])
        qsel = sb("qsel", [P, P], bf16)
        nid = sb("nid", [P, NT])
        x_nm = sb("x_nm", [P, NT, F])
        x1_nm = sb("x1_nm", [P, NT, F])
        idx_all = sb("idx_all", [P, NC + 2, NQ * J], i32)
        start_nm = sb("start_nm", [P, NT])
        end_nm = sb("end_nm", [P, NT])
        has_nm = sb("has_nm", [P, NT])
        hasb_nm = sb("hasb_nm", [P, NT])
        cross_nm = sb("cross_nm", [P, NT, 3])
        last_nm = sb("last_nm", [P, NT], i32)
        scat_nm = sb("scat_nm", [P, NT], i32)
        tmp_a = sb("tmp_a", [P, NT])
        tmp_b = sb("tmp_b", [P, NT])
        wide = sb("wide", [P, 1617])
        edge_i = sb("edge_i", [P, 38], i32)
        tail_f = sb("tail_f", [1, P])
        headidx = sb("headidx", [NQ, 1], i32)
        headrow = sb("headrow", [NQ, ROW])
        w_in = [sb(f"w_in{l}", [F, F]) for l in range(3)]
        w_rep = [sb(f"w_rep{l}", [F, NQ, F]) for l in range(3)]
        w_att = [sb(f"w_att{l}", [F, ROW]) for l in range(3)]
        att_col = [sb(f"att_col{l}", [P, 1]) for l in range(3)]
        w_as = [sb(f"w_as{l}", [P, P]) for l in range(3)]
        same_head = [sb(f"same_head{h}", [P, P]) for h in (1, 2)]
        ad_sel = sb("ad_sel", [F, J, P])
        w_node = [sb(f"w_node{l}", [P, 4, ROW]) for l in range(3)]
        bias = [sb(f"bias{l}", [P, F]) for l in range(3)]
        bias2 = sb("bias_mlp", [P, F])
        ea_s = sb("ea_s", [P, 4])
        w_hid = sb("w_hid", [P, 3, 2, P])
        w_out = sb("w_out", [P, 2, P])
        b_hid = sb("b_hid", [P, 1])

        dt_ = sb("dt_", [HALF, 8, L + 1], i32)
        st_ = sb("st_", [HALF, 8, L], i32)
        rbf = sb("rbf", [HALF, 8, L], bf16)
        d0i = sb("d0i", [112, TU], i32)
        d0f = sb("d0f", [112, TU])
        rowbuf = sb("rowbuf", [P, 2, TU, L], i32)
        rowidx = sb("rowidx", [P, 2, TU], i32)
        nid_half = sb("nid_half", [P, NT])
        sign_sum = sb("sign_sum", [P, NT])
        cnt_a = sb("cnt_a", [P, 2, TU])
        cnt_b = sb("cnt_b", [P, 2, TU])

        idx = [sb(f"idx{b}", [P, NQ * J], i32) for b in range(2)]
        g = [sb(f"g{b}", [P, NQ * J, F]) for b in range(2)]
        ad = [sb(f"ad{b}", [P, NQ, J, 2]) for b in range(2)]
        adt_sb = sb("adt_sb", [F, P])
        h_sb = sb("h_sb", [P, L])
        r_in = [sb(f"r_in{b}", [NQ, L], bf16) for b in range(2)]
        r_sb = [sb(f"r_sb{b}", [P, L]) for b in range(2)]
        adf = [sb(f"adf{b}", [P, L]) for b in range(2)]
        u_sb = sb("u_sb", [P, L])
        lm = sb("lm", [P, 2, L])
        dif = sb("dif", [P, 2, L])
        pc = sb("pc", [P, 2, L])
        ph = sb("ph", [P, L])
        mb = [sb(f"mb{b}", [P, L + 1]) for b in range(2)]
        s_b = [sb(f"s_b{b}", [P, L]) for b in range(2)]
        d_b = [sb(f"d_b{b}", [P, L]) for b in range(2)]
        o_sb = [sb(f"o_sb{b}", [P, NQ, J, OW]) for b in range(2)]
        ea_in = [lm[:, 0, :].rearrange("p (q k) -> p q k", q=NQ), dif[:, 0, :].rearrange("p (q k) -> p q k", q=NQ)]
        xd_in = [lm[:, 1, :].rearrange("p (q k) -> p q k", q=NQ), dif[:, 1, :].rearrange("p (q k) -> p q k", q=NQ)]
        xs_t, xe_t = pc[:, 0, :], pc[:, 1, :]
        hid = d_b
        ea_by_j, xd_by_j = u_sb, ph

        gidx = [sb(f"gidx{b}", [P, TU], i32) for b in range(2)]
        sidx = [sb(f"sidx{b}", [P, TU], i32) for b in range(2)]
        ng = [sb(f"ng{b}", [P, TU, OW]) for b in range(2)]
        ends = sb("ends", [P, 3, OW])
        m4 = sb("m4", [P, 4, TU, 2])
        nm = sb("nm", [P, TU, 2])
        w4 = sb("w4", [P, 4, TU, 2])
        d4 = sb("d4", [P, 4, TU, 2])
        dn = sb("dn", [P, TU, 2])
        k4 = sb("k4", [P, 4, TU, 2])
        z = sb("z", [P, TU, F])
        z2 = sb("z2", [P, TU, F])
        e_sb = sb("e_sb", [P, TU, F])
        row1 = sb("row1", [P, TU])
        row2 = sb("row2", [P, TU])
        std = sb("std", [P, TU])
        xn = [sb(f"xn{b}", [P, TU, F]) for b in range(2)]
        xt = sb("xt", [P, 2, P])
        th = [sb(f"th{b}", [P, TU, F]) for b in range(2)]
        td = [sb(f"td{b}", [P, TU, 2]) for b in range(2)]

        bank = [ctx.enter_context(nc.psum_tensor(f"bank{k}", [P, 512], fp32)) for k in range(8)]
        p_h, p_as, p_ad, p_r, p_s, p_dm, p_adt = bank[0:2], bank[2], bank[3], bank[4], bank[5], bank[6], bank[7]
        p_xs, p_xe, p_xd, p_hid, p_v, p_o = bank[0], bank[1], bank[2], (bank[3], bank[5]), bank[6], bank[7]
        p_t, p_n = bank[0], bank[1]

        S = {n: sem("q_" + n) for n in (
            "edge", "pads", "scat", "const", "par", "blk", "cast", "pad", "wide", "fill", "src", "tiles", "dve", "rw", "hd", "d0", "act0",
            "xload", "startw", "endr", "wrep", "wnode", "tickp", "tickv", "samples", "sums", "ticks", "tickt", "aidx", "row0", "row1",
            "cnta", "cntb", "idx0", "pdiag", "pbc", "ptr", "ready", "wpe", "ticks2", "tickl")}
        E = {n: sem("e_" + n) for n in (
            "ld0", "ld1", "pin", "pout", "rs", "adt", "ht", "exp", "aout", "dve", "st0", "st1")}
        e_g = [[sem(f"e_g{b}{j}") for j in range(J)] for b in range(2)]
        M = {n: sem("m_" + n) for n in (
            "ld0", "ld1", "pin", "phid", "pv", "pout", "rs", "xs", "xe", "re", "fill", "rel0", "rel1", "aout", "scan", "st0", "st1")}
        D = {n: sem("n_" + n) for n in (
            "gidx", "sidx", "g0", "g1", "s0", "s1", "ends", "dif", "exp", "zmin", "zexp", "var", "std", "xn", "pt", "xt", "pn",
            "tb", "tst0", "tst1", "chain", "head", "headw", "out")}

        def tick(eng, which):
            eng.sem_inc(S[which], 1)

        block = ctx.enter_context(nc.Block())
        done_st = lambda layer: (layer + 1) * (NC // 2) * 16
        N_PAR = 3 * 2 + 3 * 2 + 3 * 4 + 2 + 2 + 12 + 4
        TST = [k * NU // 2 * 32 for k in range(4)] + [3 * NU // 2 * 32 + NU // 2 * 16]
        CHAIN = (0, 21, 19, 25, 17)

        @block.sync
        def _(eng):
            n_par = [0]

            def par(o, i):
                eng.dma_start(o, i).then_inc(S["par"], 16)
                n_par[0] += 1

            eng.wait_ge(S["edge"], 1)
            whole, rest = divmod(N_EDGES // L, TU)
            eng.dma_start(d0i[0:whole, :], bass.AP(tensor=I["dst"].tensor, offset=0, ap=[[TU * L, whole], [L, TU]])).then_inc(S["d0"], 16)
            eng.dma_start(d0i[whole:whole + 1, 0:rest + 1],
                          bass.AP(tensor=I["dst"].tensor, offset=whole * TU * L, ap=[[TU * L, 1], [L, rest + 1]])).then_inc(S["d0"], 16)
            eng.dma_start(dstp[LEAD:LEAD + N_EDGES].rearrange("(a b) -> a b", a=P),
                          I["dst"].rearrange("(a b) -> a b", a=P)).then_inc(S["pad"], 16)
            assert EP - N_EDGES == P * 11
            eng.dma_start(dstp[LEAD + N_EDGES:].rearrange("(a b) -> a b", b=11), edge_i[:, 0:11]).then_inc(S["pad"], 16)
            eng.dma_start(dstp[LEAD - 16:LEAD].rearrange("(a b) -> a b", a=1), edge_i[0:1, 11:27]).then_inc(S["pad"], 16)
            eng.wait_ge(S["pad"], 16 * 3)
            eng.dma_start(srcp[0:N_EDGES].rearrange("(a b) -> a b", a=P),
                          I["src"].rearrange("(a b) -> a b", a=P)).then_inc(S["pads"], 16)
            eng.dma_start(srcp[N_EDGES:].rearrange("(a b) -> a b", b=11), edge_i[:, 27:38]).then_inc(S["pads"], 16)
            for k in range(8):
                at = k * HALF * L
                eng.dma_start(dt_[:, k, :], bass.AP(tensor=dstp.tensor, offset=LEAD + at - 1, ap=[[L, HALF], [1, L + 1]]))\
                   .then_inc(S["tiles"], 16)
            eng.wait_ge(S["pads"], 32)
            for k in range(8):
                eng.dma_start(st_[:, k, :], srcp[k * HALF * L:(k + 1) * HALF * L].rearrange("(c l) -> c l", l=L))\
                   .then_inc(S["src"], 16)
            eng.dma_start(headidx[:, :], bass.AP(tensor=dstp.tensor, offset=LEAD, ap=[[Q, NQ], [1, 1]])).then_inc(S["hd"], 16)
            eng.wait_ge(S["const"], 4)
            for l in range(3):
                par(w_in[l][:, :], I[f"L0_gnn_W{l + 1}"])
                par(bias[l][:, :], I[f"L0_gnn_b{l + 1}"].partition_broadcast(P))
                att_s, att_d = I[f"L0_gnn_att_s{l + 1}"], I[f"L0_gnn_att_d{l + 1}"]
                heads, ch = att_d.shape
                for q in range(NQ):
                    par(att_col[l][q * F:(q + 1) * F, :], att_s.rearrange("a (c b) -> (a c) b", b=1))
                for h in range(2):
                    o = w_att[l][h * ch:(h + 1) * ch, F + h:F + h + 1] if heads == 2 else w_att[l][:, F + h:F + h + 1]
                    par(o, att_d[h % heads:h % heads + 1, :].rearrange("a c -> c a"))
            par(bias2[:, :], I["L1_gnn_b2"].partition_broadcast(P))
            par(ea_s[:, 0:1], I["L0_gnn_ea1"].partition_broadcast(P))
            for half in range(2):
                par(b_hid[half * HID:(half + 1) * HID, :], I["L1_gnn_b1"].rearrange("(a b) -> a b", b=1))
                for q in range(2):
                    s = 2 * half + q
                    for k in range(3):
                        par(w_hid[s * F:(s + 1) * F, k, half, q * HID:(q + 1) * HID], I["L1_gnn_W1"][k * F:(k + 1) * F, :])
                    par(w_out[q * HID:(q + 1) * HID, half, s * F:(s + 1) * F], I["L1_gnn_W2"])
            assert n_par[0] == N_PAR, n_par
            for a, b in ((0, 112), (112, P - 1)):
                eng.dma_start(x_nm[a:b, :, :].rearrange("p t f -> p (t f)"),
                              I["x"][a * NT:b * NT, :].rearrange("(p t) f -> p (t f)", t=NT)).then_inc(S["xload"], 16)
            eng.dma_start(x_nm[P - 1:P, 0:LAST_P, :].rearrange("p t f -> p (t f)"),
                          I["x"][(P - 1) * NT:, :].rearrange("(p t) f -> p (t f)", p=1)).then_inc(S["xload"], 16)
            for k in range(4):
                eng.dma_start(aux[:, :].rearrange("(p e) c -> p (e c)", p=P)[:, k * 1617:(k + 1) * 1617], wide[:, :]).then_inc(S["fill"], 16)
            eng.wait_ge(S["ready"], 1)
            eng.dma_start(startd[0:NP].rearrange("(p t) -> p t", t=NT), start_nm[:, :]).then_inc(S["startw"], 16)
            eng.dma_start(startd[NP:].rearrange("(a b) -> a b", a=1), tail_f[:, :]).then_inc(S["startw"], 16)
            eng.wait_ge(S["startw"], 32)
            eng.dma_start(end_nm[:, :], startd[1:NP + 1].rearrange("(p t) -> p t", t=NT)).then_inc(S["endr"], 16)
            eng.wait_ge(S["rw"], 1)
            for k in range(8):
                eng.dma_start(rrow[k * HALF * L:(k + 1) * HALF * L].rearrange("(c l) -> c l", l=L), rbf[:, k, :]).then_inc(S["rw"], 16)

            def load_gat(layer, v, b):
                n = layer * NC + v
                need(eng, E["pin"], (n - 2) * 5 + 2)
                tick(eng, "tickl")
                eng.dma_start(ad[b][:, :, :, :].rearrange("p q j c -> p q (j c)"),
                              aux[0:EP, :].rearrange("(q c p j) h -> c p q (j h)", q=NQ, c=NC, p=P)[v, :, :, :] if isinstance(v, int) else
                              aux[0:EP, :].rearrange("(q c p j) h -> c p q (j h)", q=NQ, c=NC, p=P)[bass.ds(v, 1), :, :, :].rearrange("c p q k -> p (c q) k"))\
                   .then_inc(E[f"ld{b}"], 16)
                load_r(v, b, E[f"ld{b}"])

            def load_r(v, b, s):
                rv = rrow.rearrange("(q e) -> q e", q=NQ)
                eng.dma_start(r_in[b][:, :], rv[:, v * L:(v + 1) * L] if isinstance(v, int) else rv[:, bass.ds(v * L, L)]).then_inc(s, 16)

            def store_gat(layer, v, b):
                n = layer * NC + v
                need(eng, E["aout"], (n + 1) * 2)
                tick(eng, "tickl")
                sv = state.rearrange("(q c p j) w -> c p q (j w)", q=NQ, c=NC, p=P)
                dst = sv[v, :, :, :] if isinstance(v, int) else sv[bass.ds(v, 1), :, :, :].rearrange("c p q k -> p (c q) k")
                eng.dma_start(dst, o_sb[b][:, :, :, :].rearrange("p q j w -> p q (j w)")).then_inc(E[f"st{b}"], 16)

            wide_v = auxx.rearrange("(p e) c -> p (e c)", p=P)

            def node(step):
                n0 = step * NU
                if step:
                    if step < 4:
                        src = bass.AP(tensor=state.tensor, offset=(Q - 1) * OW, ap=[[0, P], [Q * OW, 3], [1, OW]])
                        for b in range(2):
                            eng.wait_ge(E[f"st{b}"], done_st(step - 1))
                        eng.dma_start(ends[:, :, :], src).then_inc(D["ends"], 16)
                    else:
                        src = bass.AP(tensor=vmax.tensor, offset=(Q - 1) * F, ap=[[0, P], [Q * F, 3], [1, F]])
                        for b in range(2):
                            eng.wait_ge(M[f"st{b}"], done_st(0))
                        eng.dma_start(ends[:, :, 0:F], src).then_inc(D["ends"], 16)
                if step == 4:
                    return
                tv = table.rearrange("(p t) c -> p (t c)", t=NT)
                w = F * TU

                def store(u, b):
                    if step < 3:
                        need(eng, D["tb"], n0 + u + 1)
                        tick(eng, "tickl")
                        src = th[b][:, :, :].rearrange("p t c -> p (t c)")
                        av = adtable.rearrange("(p t) c -> p (t c)", t=NT)
                        eng.dma_start(av[:, u * (2 * TU):(u + 1) * (2 * TU)] if isinstance(u, int) else av[:, bass.ds(u * (2 * TU), 2 * TU)],
                                      td[b][:, :, :].rearrange("p t c -> p (t c)")).then_inc(D[f"tst{b}"], 16)
                    else:
                        need(eng, D["xn"], n0 + u + 1)
                        tick(eng, "tickl")
                        src = xn[b][:, :, :].rearrange("p t c -> p (t c)")
                    eng.dma_start(tv[:, u * w:(u + 1) * w] if isinstance(u, int) else tv[:, bass.ds(u * w, w)], src)\
                       .then_inc(D[f"tst{b}"], 16)

                with eng.Fori(0, NU // 2) as i:
                    store(i * 2, 0)
                    store(i * 2 + 1, 1)
                eng.wait_ge(D["head"], 16 * (step + 1))
                for b in range(2):
                    eng.wait_ge(D[f"s{b}"], (step + 1) * NU // 2 * TU * 16)
                if step < 3:
                    eng.dma_start(bass.AP(tensor=aux.tensor, offset=0, ap=[[2 * Q, NQ], [1, 2]]), headrow[:, 0:2])\
                       .then_inc(D["headw"], 16)
                else:
                    eng.dma_start(bass.AP(tensor=auxx.tensor, offset=0, ap=[[F * Q, NQ], [1, F]]), headrow[:, 0:F])\
                       .then_inc(D["headw"], 16)
                eng.wait_ge(D["headw"], 16 * (step + 1))

            for layer in range(3):
                node(layer)
                if layer == 0:
                    eng.wait_ge(S["rw"], 1 + 16 * 8)
                load_gat(layer, 0, 0)
                load_gat(layer, 1, 1)

                def steps(v, b):
                    if not isinstance(v, int) or v + 2 < NC:
                        load_gat(layer, v + 2, b)
                    store_gat(layer, v, b)

                def fill_x(i):
                    if layer == 0:
                        w = EL * F // P // (NC // 2)
                        eng.dma_start(wide_v[:, i * w:(i + 1) * w] if isinstance(i, int) else wide_v[:, bass.ds(i * w, w)],
                                      wide[:, 0:w]).then_inc(S["wide"], 16)
                steps(0, 0)
                steps(1, 1)
                fill_x(0)
                with eng.Fori(1, NC // 2 - 1) as i:
                    steps(i * 2, 0)
                    steps(i * 2 + 1, 1)
                    fill_x(i)
                steps(NC - 2, 0)
                steps(NC - 1, 1)
                fill_x(NC // 2 - 1)
            node(3)

            def load_mlp(v, b):
                need(eng, M["pin"], (v - 2) * 2 + 1)
                tick(eng, "tickl")
                need(eng, M["re"], v - 1)
                tick(eng, "tickl")
                load_r(v, b, M[f"ld{b}"])
                av = auxx[0:EP, :].rearrange("(q c p j) f -> c p q (j f)", q=NQ, c=NC, p=P)
                eng.dma_start(xd_in[b][:, :, :], av[v, :, :, :] if isinstance(v, int) else
                              av[bass.ds(v, 1), :, :, :].rearrange("c p q k -> p (c q) k")).then_inc(M[f"ld{b}"], 16)
                ev = I["edge_attr_32"].rearrange("e f -> (e f)")
                for q in range(NQ):
                    rows = P
                    if isinstance(v, int):
                        rows = max(0, min(P, (N_EDGES - q * Q - v * L) // J))
                    rows, at = (P, 0) if rows == 0 else (rows, v * (L * F) + q * Q * F)
                    o = ea_in[b][0:rows, q, :]
                    if isinstance(at, int):
                        i_ = bass.AP(tensor=I["edge_attr_32"].tensor, offset=at, ap=[[J * F, rows], [1, J * F]])
                    else:
                        i_ = ev[bass.ds(at, L * F)].rearrange("(p k) -> p k", p=P)
                    eng.dma_start(o, i_).then_inc(M[f"ld{b}"], 16)

            def store_mlp(v, b):
                need(eng, M["aout"], v + 1)
                tick(eng, "tickl")
                sv = vmax.rearrange("(q c p j) w -> c p q (j w)", q=NQ, c=NC, p=P)
                dst = sv[v, :, :, :] if isinstance(v, int) else sv[bass.ds(v, 1), :, :, :].rearrange("c p q k -> p (c q) k")
                eng.dma_start(dst, view(o_sb[b], 0, [[J * F, NQ], [1, J * F]])).then_inc(M[f"st{b}"], 16)

            load_mlp(0, 0)
            load_mlp(1, 1)
            for v in (0, 1):
                load_mlp(v + 2, v)
                store_mlp(v, v)
            with eng.Fori(1, NC // 2 - 3) as i:
                for b in range(2):
                    load_mlp(i * 2 + (b + 2), b)
                    store_mlp(i * 2 + b, b)
            for v in range(NC - 6, NC):
                if v + 2 < NC:
                    load_mlp(v + 2, v % 2)
                store_mlp(v, v % 2)
            node(4)
            eng.wait_ge(D["xn"], 5 * NU)
            for a, b in ((0, 112), (112, P - 1)):
                eng.dma_start(out[a * NT:b * NT, :].rearrange("(p t) f -> p (t f)", t=NT),
                              x1_nm[a:b, :, :].rearrange("p t f -> p (t f)")).then_inc(D["out"], 16)
            eng.dma_start(out[(P - 1) * NT:, :].rearrange("(p t) f -> p (t f)", p=1),
                          x1_nm[P - 1:P, 0:LAST_P, :].rearrange("p t f -> p (t f)")).then_inc(D["out"], 16)
            eng.wait_ge(D["out"], 48)
            eng.wait_ge(S["fill"], 64)
            eng.wait_ge(S["wide"], NC // 2 * 16)
            for b in range(2):
                eng.wait_ge(M[f"st{b}"], done_st(0))
                eng.wait_ge(D[f"tst{b}"], TST[4])

        @block.gpsimd
        def _(eng):
            eng.memset(d0i[:, :], N_NODES)
            eng.memset(edge_i[:, 0:11], N_NODES)
            eng.memset(edge_i[:, 11:27], -1)
            eng.memset(edge_i[:, 27:38], 0).then_inc(S["edge"], 1)
            eng.memset(ident[:, :], 0.0).then_inc(S["blk"], 1)
            eng.memset(qsel[:, :], 0.0).then_inc(S["blk"], 1)
            eng.memset(ones[:, :], 1.0)
            eng.memset(wide[:, :], -BIG).then_inc(S["const"], 1)
            eng.memset(tail_f[:, :], float(EP)).then_inc(S["const"], 1)
            eng.iota(nid[:, :], pattern=[[1, NT]], base=0, channel_multiplier=NT,
                     allow_small_or_imprecise_dtypes=True).then_inc(S["const"], 1)
            eng.memset(same_head[1][:, :], 1.0)
            eng.memset(ad_sel[:, :, :], 0.0)
            eng.memset(same_head[0][:, :], 0.0).then_inc(S["blk"], 1)
            for t in [w_hid, w_out] + w_att:
                eng.memset(t[tuple([slice(None)] * len(t.shape))], 0.0)
            eng.memset(x_nm[:, :, :], 0.0)
            eng.memset(headrow[:, :], 0.0).then_inc(S["const"], 1)
            eng.wait_ge(S["blk"], 3)
            eng.affine_select(out=ident[:, :], in_=ident[:, :], compare_op=ALU.not_equal, fill=1.0,
                              base=0, pattern=[[-1, P]], channel_multiplier=1).then_inc(S["blk"], 1)
            eng.affine_select(out=qsel[:, :].rearrange("p (q f) -> p q f", q=NQ),
                              in_=qsel[:, :].rearrange("p (q f) -> p q f", q=NQ), compare_op=ALU.not_equal, fill=1.0,
                              base=0, pattern=[[-1, NQ], [0, F]], channel_multiplier=1).then_inc(S["blk"], 1)
            for j in range(J):
                o = ad_sel[:, j, :].rearrange("k (q h i) -> k q h i", q=NQ, h=2)
                eng.affine_select(out=o, in_=o, compare_op=ALU.not_equal, fill=1.0, base=-2 * j,
                                  pattern=[[-2 * J, NQ], [-1, 2], [0, 16]], channel_multiplier=1)
            o = same_head[1][:, :].rearrange("p (a i) -> p a i", i=16)
            eng.affine_select(out=o, in_=o, compare_op=ALU.is_ge, fill=0.0, base=0,
                              pattern=[[-16, 8], [0, 16]], channel_multiplier=1).then_inc(S["blk"], 1)
            eng.wait_ge(S["blk"], 6)
            eng.affine_select(out=o, in_=o, compare_op=ALU.is_ge, fill=0.0, base=15,
                              pattern=[[16, 8], [0, 16]], channel_multiplier=-1).then_inc(S["blk"], 1)

            dst_rows = dstp.rearrange("(s l) -> s l", l=L)

            def search(u, b):
                need(eng, S["cnta"], u + 1)
                need(eng, S["cntb"], u - 1)
                tick(eng, "tickp")
                for t in range(TU):
                    eng.indirect_dma_start(rowbuf[:, b, t, :], None, dst_rows,
                                           bass.IndirectOffsetOnAxis(ap=rowidx[:, b, t:t + 1], axis=0)).then_inc(S[f"row{b}"], 16)

            eng.wait_ge(S["pad"], 16 * 3)
            search(0, 0)
            search(1, 1)
            with eng.Fori(1, NU // 2) as i:
                search(i * 2, 0)
                search(i * 2 + 1, 1)

            def gather_nodes(step, u, b):
                n = (step - 1) * NU + u
                need(eng, D["gidx"], n + 1)
                need(eng, D["xn"], step * NU + u - 1)
                tick(eng, "tickp")
                src = state if step < 4 else vmax
                for t in range(TU):
                    eng.indirect_dma_start(ng[b][:, t, 0:(OW if step < 4 else F)], None, src[:, :],
                                           bass.IndirectOffsetOnAxis(ap=gidx[b][:, t:t + 1], axis=0)).then_inc(D[f"g{b}"], 16)

            def scatter_nodes(step, u, b):
                n = step * NU + u
                need(eng, D["sidx"], n + 1)
                if step < 3:
                    need(eng, D["tb"], n + 1)
                else:
                    need(eng, D["xn"], n + 1)
                tick(eng, "tickp")
                for t in range(TU):
                    o, i_ = (aux, td[b][:, t, :]) if step < 3 else (auxx, xn[b][:, t, :])
                    eng.indirect_dma_start(o[:, :], bass.IndirectOffsetOnAxis(ap=sidx[b][:, t:t + 1], axis=0),
                                           i_, None).then_inc(D[f"s{b}"], 16)

            def node(step):
                if step:
                    for b in range(2):
                        if step < 4:
                            eng.wait_ge(E[f"st{b}"], done_st(step - 1))
                        else:
                            eng.wait_ge(M[f"st{b}"], done_st(0))
                if step == 0:
                    eng.wait_ge(S["fill"], 64)
                if step == 3:
                    eng.wait_ge(S["wide"], NC // 2 * 16)
                if step == 4:
                    gather_nodes(step, 0, 0)
                    gather_nodes(step, 1, 1)
                    with eng.Fori(1, NU // 2) as i:
                        gather_nodes(step, i * 2, 0)
                        gather_nodes(step, i * 2 + 1, 1)
                    return
                if step:
                    gather_nodes(step, 0, 0)
                    with eng.Fori(0, NU // 2 - 1) as i:
                        gather_nodes(step, i * 2 + 1, 1)
                        scatter_nodes(step, i * 2, 0)
                        gather_nodes(step, i * 2 + 2, 0)
                        scatter_nodes(step, i * 2 + 1, 1)
                    gather_nodes(step, NU - 1, 1)
                    scatter_nodes(step, NU - 2, 0)
                    scatter_nodes(step, NU - 1, 1)
                else:
                    with eng.Fori(0, NU // 2) as i:
                        scatter_nodes(step, i * 2, 0)
                        scatter_nodes(step, i * 2 + 1, 1)
                for b in range(2):
                    eng.wait_ge(D[f"tst{b}"], TST[step + 1])
                if step == 0:
                    eng.wait_ge(S["hd"], 16)
                t, w = (adtable, 2) if step < 3 else (table, F)
                if step:
                    eng.wait_ge(D["headw"], 16 * step)
                eng.indirect_dma_start(headrow[:, 0:w], None, t[:, :],
                                       bass.IndirectOffsetOnAxis(ap=headidx[:, 0:1], axis=0)).then_inc(D["head"], 16)

            def gather_edges(n, v, b, progress, k):
                need(eng, S["aidx"], n + 1)
                need(eng, progress, k)
                tick(eng, "tickp")
                for j in range(J):
                    for q in range(NQ - 1 if isinstance(v, int) and v >= NC - 2 else NQ):
                        eng.indirect_dma_start(g[b][:, j * NQ + q, :], None, table[:, :],
                                               bass.IndirectOffsetOnAxis(ap=idx[b][:, q * J + j:q * J + j + 1], axis=0)).then_inc(e_g[b][j], 16)

            for layer in range(3):
                node(layer)

                def gat(v, b):
                    n = layer * NC + v
                    gather_edges(n, v, b, E["pin"], (n - 2) * 5 + 4)
                gat(0, 0)
                gat(1, 1)
                with eng.Fori(1, NC // 2 - 1) as i:
                    gat(i * 2, 0)
                    gat(i * 2 + 1, 1)
                gat(NC - 2, 0)
                gat(NC - 1, 1)
            node(3)

            def mlp(v, b):
                gather_edges(3 * NC + v, v, b, M["pin"], (v - 1) * 2)
            mlp(0, 0)
            mlp(1, 1)
            with eng.Fori(1, NC // 2 - 1) as i:
                mlp(i * 2, 0)
                mlp(i * 2 + 1, 1)
            mlp(NC - 2, 0)
            mlp(NC - 1, 1)
            node(4)

        def gathered(pass_, v, b):
            last = 16 if isinstance(v, int) and v >= NC - 2 else 0
            return pass_ * (NC // 2 * 64 - 16) + (v * 32 + (64 - 32 * b - last))

        @block.tensor
        def _(eng):
            eng.wait_ge(S["blk"], 7)
            eng.wait_ge(S["pdiag"], 1)
            for k, (a, b) in enumerate(((0, 4), (4, TU))):
                eng.matmul(bank[k][:, 0:(b - a) * 112], ones[0:112, :], view(x1_nm, a * 112, [[1, (b - a) * 112]], parts=112),
                           start=True, stop=True).then_inc(S["pbc"], 1)
            eng.wait_ge(S["wrep"], 1)
            for l in range(3):
                eng.matmul(bank[2 + l][:, 0:ROW], w_rep[l][:, :, :].rearrange("o a k -> o (a k)"), w_att[l][:, :],
                           start=True, stop=True).then_inc(S["wpe"], 1)
            eng.wait_ge(S["cast"], 1)
            eng.wait_ge(S["wnode"], 1)
            for k in range(8):
                for j in range(J):
                    last = eng.transpose(bank[k][:, j * HALF:(j + 1) * HALF],
                                         view(st_, k * L + j, [[J, P]], parts=HALF).bitcast(fp32),
                                         ident[0:HALF, 0:HALF])
                last.then_inc(S["ptr"], 1)
            eng.wait_ge(S["idx0"], 8)

            def node(step):
                def rows(u, b):
                    n = step * NU + u
                    need(eng, D["xn"], n + 1)
                    need(eng, D["xt"], n)
                    for k, t in enumerate((0, TU - 4)):
                        last = eng.transpose(p_t[:, k * P:(k + 1) * P],
                                             xn[b][:, t:t + 4, :].rearrange("p t f -> p (t f)"), ident[:, :])
                    last.then_inc(D["pt"], 1)
                    need(eng, D["xt"], n + 1)
                    need(eng, D["tb"], n)
                    for k in range(2):
                        last = eng.matmul(p_n[:, k * 4 * ROW:(k + 1) * 4 * ROW], xt[:, k, :],
                                          w_node[step][:, :, :].rearrange("p t c -> p (t c)"), start=True, stop=True)
                    last.then_inc(D["pn"], 1)

                rows(0, 0)
                rows(1, 1)
                with eng.Fori(1, NU // 2) as i:
                    rows(i * 2, 0)
                    rows(i * 2 + 1, 1)

            def restart_row(b):
                return eng.matmul(p_r[:, :], qsel[0:NQ, :], r_in[b][:, :], start=True, stop=True)

            def cols(t, j):
                return view(t, j, [[J, P]])

            for layer in range(3):
                node(layer)

                def front(v, b):
                    n = layer * NC + v
                    need(eng, E[f"ld{b}"], (layer * NC // 2) * 32 + (v * 16 + (32 - 16 * b)))
                    need(eng, E["rs"], n)
                    tick(eng, "tickt")
                    restart_row(b).then_inc(E["pin"], 1)
                    need(eng, E["adt"], n)
                    eng.transpose(p_adt[0:F, 0:P], ad[b][:, :, :, :].rearrange("p q j h -> p (q j h)"), ident[:, :]).then_inc(E["pin"], 1)
                    need(eng, E["adt"], n + 1)
                    need(eng, E["dve"], (n - 1) * 10 + 1)
                    tick(eng, "tickt")
                    for j in range(J):
                        last = eng.matmul(cols(p_ad, j), ad_sel[:, j, :], adt_sb[:, :], start=True, stop=True)
                    last.then_inc(E["pin"], 1)

                def hidden(v, b):
                    n = layer * NC + v
                    need(eng, E["dve"], (n - 2) * 10 + 8)
                    for j in range(J):
                        eng.wait_ge(e_g[b][j], gathered(layer, v, b))
                        last = eng.transpose(cols(p_h[b], j), view(g[b], j * P, [[1, P]]), ident[:, :])
                    last.then_inc(E["pin"], 1)
                    need(eng, E["ht"], n + 1)
                    need(eng, E["dve"], (n - 1) * 10 + 2)
                    eng.matmul(p_as[:, :], w_as[layer][:, :], h_sb[:, :], start=True, stop=True).then_inc(E["pin"], 1)

                def back(v, b):
                    n = layer * NC + v
                    need(eng, E["aout"], (n - 1) * 2 + 1)
                    need(eng, E["dve"], n * 10 + 9)
                    for j in range(J):
                        last = eng.transpose(p_s[:, j * P:(j + 1) * P], cols(s_b[b], j), ident[:, :])
                    last.then_inc(E["pout"], 1)
                    need(eng, E["aout"], n * 2)
                    need(eng, E["dve"], n * 10 + 10)
                    for j in range(J):
                        for k, lhs in ((0, cols(d_b[b], j)), (2, view(mb[b], j + 1, [[J, P]]))):
                            last = eng.matmul(view(p_dm, 16 * j + k, [[4, NQ], [1, 2]]), lhs, view(ident, 0, [[F, NQ], [16, 2]]),
                                              start=True, stop=True)
                    last.then_inc(E["pout"], 1)

                front(0, 0)
                hidden(0, 0)
                front(1, 1)
                back(0, 0)
                hidden(1, 1)
                with eng.Fori(1, NC // 2 - 1) as i:
                    for b in range(2):
                        front(i * 2 + b, b)
                        back(i * 2 + (b - 1), 1 - b)
                        hidden(i * 2 + b, b)
                for v in (NC - 2, NC - 1):
                    front(v, v % 2)
                    back(v - 1, 1 - v % 2)
                    hidden(v, v % 2)
                back(NC - 1, 1)
            eng.wait_ge(E["aout"], 3 * NC * 2)
            def front(v, b):
                need(eng, M[f"ld{b}"], v * 48 + (96 - 48 * b))
                need(eng, M["rs"], v)
                tick(eng, "tickt")
                restart_row(b).then_inc(M["pin"], 1)
                need(eng, M["fill"], v)
                need(eng, M["xe"], v)
                need(eng, M["re"], v + 1)
                for j in range(J):
                    eng.transpose(cols(p_xd, j), view(xd_by_j, j * P, [[1, P]]), ident[:, :])
                    eng.transpose(cols(p_xe, j), view(ea_by_j, j * P, [[1, P]]), ident[:, :])
                need(eng, M["xs"], v)
                for j in range(J):
                    eng.wait_ge(e_g[b][j], gathered(3, v, b))
                    last = eng.transpose(cols(p_xs, j), view(g[b], j * P, [[1, P]]), ident[:, :])
                last.then_inc(M["pin"], 1)

            def middle(v, b):
                need(eng, M["fill"], v + 1)
                need(eng, M["xe"], v + 1)
                need(eng, M["xs"], v + 1)
                for h in range(2):
                    need(eng, M[f"rel{h}"], v)
                    for k, t in enumerate((xs_t, adf[b][:, :], xe_t)):
                        last = eng.matmul(p_hid[h][:, :], w_hid[:, k, h, :], t, start=(k == 0), stop=(k == 2))
                    last.then_inc(M["phid"], 1)
                need(eng, M["scan"], v)
                for h in range(2):
                    need(eng, M[f"rel{h}"], v + 1)
                    last = eng.matmul(p_v[:, :], w_out[:, h, :], hid[h][:, :], start=(h == 0), stop=(h == 1))
                last.then_inc(M["pv"], 1)

            def back(v, b):
                need(eng, M["scan"], v + 1)
                need(eng, M["aout"], v)
                for j in range(J):
                    last = eng.transpose(p_o[:, j * P:(j + 1) * P], cols(s_b[b], j), ident[:, :])
                last.then_inc(M["pout"], 1)

            def chunk(v, b):
                middle(v, b)
                back(v - 1, 1 - b)
                front(v + 1, 1 - b)

            front(0, 0)
            middle(0, 0)
            front(1, 1)
            chunk(1, 1)
            with eng.Fori(1, NC // 2 - 2) as i:
                chunk(i * 2, 0)
                chunk(i * 2 + 1, 1)
            for v in (NC - 4, NC - 3, NC - 2):
                chunk(v, v % 2)
            middle(NC - 1, 1)
            back(NC - 2, 0)
            back(NC - 1, 1)

        @block.scalar
        def _(eng):
            def copy(o, i):
                return eng.activation(o, i, ACT.Copy)

            eng.wait_ge(S["samples"], 1)
            with eng.Fori(0, NU) as i:
                for t in range(TU):
                    one = lambda x: x[:, bass.ds(i * TU + t, 1)]
                    eng.activation(view(x1_nm, 2 * SAMPLES, [[1, SAMPLES]]), view(x1_nm, SAMPLES, [[1, SAMPLES]]), ACT.Sign,
                                   scale=-1.0, bias=one(nid_half), accum_out=one(sign_sum)).then_inc(S["sums"], 1)
                    eng.wait_ge(S["sums"], i * TU + (t + 1))
            for k in range(8):
                q, half = k // 2, k % 2
                eng.wait_ge(S["ptr"], k + 1)
                copy(view(idx_all, (half * HALF) * 16 + q * J, [[16, HALF], [1, J]]),
                     view(bank[k], 0, [[1, HALF], [HALF, J]])).then_inc(S["idx0"], 1)
            eng.wait_ge(S["idx0"], 8)
            copy(idx_all[:, NC:NC + 2, :], idx_all[:, 0:2, :]).then_inc(S["idx0"], 1)
            for b in range(2):
                copy(idx[b][:, :], idx_all[:, b, :]).then_inc(S["aidx"], 1)
            eng.wait_ge(S["idx0"], 9)
            eng.wait_ge(S["par"], N_PAR * 16)
            eng.activation(ea_s[:, 1:2], ea_s[:, 0:1], ACT.Tanh).then_inc(S["act0"], 1)

            def next_idx(n, v, b, pin, k):
                need(eng, pin, k)
                tick(eng, "ticks")
                src = idx_all[:, v + 2, :] if isinstance(v, int) else idx_all[:, bass.ds(v + 2, 1), :].rearrange("p c k -> p (c k)")
                copy(idx[b][:, :], src).then_inc(S["aidx"], 1)

            def node(step):
                def indices(u, b, which):
                    t, src = (gidx, last_nm) if which == "gidx" else (sidx, scat_nm)
                    if which == "gidx":
                        need(eng, D[f"g{b}"], ((step - 1) * NU // 2) * TU * 16 + (u - b) * (TU * 8))
                    else:
                        need(eng, D[f"s{b}"], (step * NU // 2) * TU * 16 + (u - b) * (TU * 8))
                    tick(eng, "ticks")
                    copy(t[b][:, :], src[:, u * TU:(u + 1) * TU] if isinstance(u, int) else src[:, bass.ds(u * TU, TU)])\
                        .then_inc(D[which], 1)

                def math(u, b):
                    n = step * NU + u
                    m = n - NU
                    if step in (1, 2, 3):
                        need(eng, D["dif"], m + 1)
                        eng.activation(w4[:, :, :, :].rearrange("p a t h -> p (a t h)"),
                                       m4[:, :, :, :].rearrange("p a t h -> p (a t h)"), ACT.Exp).then_inc(D["exp"], 1)
                    if step in (1, 2):
                        need(eng, D["zmin"], m + 1)
                        eng.activation(e_sb[:, :, :], z2[:, :, :], ACT.Exp).then_inc(D["zexp"], 1)
                    if step in (3, 4):
                        need(eng, D["var"], (step - 3) * NU + u + 1)
                        eng.activation(std[:, :], row1[:, :], ACT.Sqrt).then_inc(D["std"], 1)
                    if step < 3:
                        need(eng, D["pt"], n + 1)
                        copy(xt[:, :, :], p_t[:, 0:2 * P].rearrange("p (a b) -> p a b", a=2)).then_inc(D["xt"], 1)
                        need(eng, D["pn"], n + 1)
                        need(eng, D[f"tst{b}"], TST[step] + (u - b) * (16 if step < 3 else 8))
                        need(eng, D[f"s{b}"], (step * NU // 2) * TU * 16 + (u - b) * (TU * 8))
                        for t, a, w in ((th, 0, F), (td, F, 2)):
                            copy(t[b][:, 0:4, :], view(p_n, a, [[ROW, 4], [1, w]]))
                            last = copy(t[b][:, 4:TU, :], view(p_n, 5 * ROW + a, [[ROW, 3], [1, w]]))
                        last.then_inc(D["tb"], 1)

                def both(u, b):
                    indices(u, b, "sidx")
                    math(u, b)

                if step == 0:
                    for u in range(2):
                        both(u, u)
                    with eng.Fori(1, NU // 2) as i:
                        both(i * 2, 0)
                        both(i * 2 + 1, 1)
                    return

                indices(0, 0, "gidx")
                indices(1, 1, "gidx")

                def skewed(u, b):
                    if step < 4:
                        indices(u, b, "sidx")
                    math(u, b)
                    if not isinstance(u, int) or u + 2 < NU:
                        indices(u + 2, b, "gidx")
                for u in range(2):
                    skewed(u, u)
                with eng.Fori(1, NU // 2 - 1) as i:
                    skewed(i * 2, 0)
                    skewed(i * 2 + 1, 1)
                for u in (NU - 2, NU - 1):
                    skewed(u, u % 2)

            for layer in range(3):
                if layer == 0:
                    eng.wait_ge(S["scat"], 1)
                node(layer)

                def front(v, b):
                    n = layer * NC + v
                    need(eng, E["pin"], n * 5 + 1)
                    need(eng, E["dve"], (n - 2) * 10 + 6)
                    copy(r_sb[b][:, :], p_r[:, :]).then_inc(E["rs"], 1)
                    need(eng, E["pin"], n * 5 + 2)
                    copy(adt_sb[:, :], p_adt[0:F, 0:P]).then_inc(E["adt"], 1)

                def hidden(v, b):
                    n = layer * NC + v
                    need(eng, E["pin"], n * 5 + 4)
                    copy(h_sb[:, :], p_h[b][:, :]).then_inc(E["ht"], 1)
                    next_idx(n, v, b, E["pin"], n * 5 + 4)

                def exps(v, b):
                    n = layer * NC + v
                    need(eng, E["dve"], n * 10 + 7)
                    eng.activation(pc[:, :, :], dif[:, :, :], ACT.Exp).then_inc(E["exp"], 1)

                def outs(v, b):
                    n = layer * NC + v
                    need(eng, E[f"st{b}"], (layer * NC // 2) * 16 + (v - b) * 8)
                    need(eng, E["pout"], n * 2 + 1)
                    copy(view(o_sb[b], 0, [[OW, J], [J * OW, NQ], [1, F]]), view(p_s, 0, [[P, J], [F, NQ], [1, F]])).then_inc(E["aout"], 1)
                    need(eng, E["pout"], n * 2 + 2)
                    copy(view(o_sb[b], F, [[OW, J], [J * OW, NQ], [1, 4]]),
                         view(p_dm, 0, [[16, J], [4, NQ], [1, 4]])).then_inc(E["aout"], 1)

                def chunk(v, b):
                    exps(v, b)
                    front(v + 1, 1 - b)
                    outs(v, b)
                    hidden(v + 1, 1 - b)
                front(0, 0)
                hidden(0, 0)
                chunk(0, 0)
                chunk(1, 1)
                with eng.Fori(1, NC // 2 - 1) as i:
                    chunk(i * 2, 0)
                    chunk(i * 2 + 1, 1)
                chunk(NC - 2, 0)
                exps(NC - 1, 1)
                outs(NC - 1, 1)
            node(3)

            def reorder(v, b):
                need(eng, M[f"ld{b}"], v * 48 + (96 - 48 * b))
                need(eng, M["pin"], v * 2)
                tick(eng, "ticks")
                for o, i_ in ((xd_by_j, xd_in[b]), (ea_by_j, ea_in[b])):
                    last = copy(view(o, 0, [[F, NQ], [P, J], [1, F]]), i_.rearrange("p q (j f) -> p q j f", j=J))
                last.then_inc(M["re"], 1)

            def rs(v, b):
                need(eng, M["pin"], v * 2 + 1)
                need(eng, M["scan"], v - 1)
                copy(r_sb[b][:, :], p_r[:, :]).then_inc(M["rs"], 1)

            def xs(v, b):
                need(eng, M["pin"], v * 2 + 2)
                need(eng, M["phid"], v * 2)
                copy(xs_t, p_xs[:, :]).then_inc(M["xs"], 1)

            def rel(v, b):
                need(eng, M["phid"], v * 2 + 1)
                need(eng, M["pv"], v)
                eng.activation(hid[0][:, :], p_hid[0][:, :], ACT.Relu, bias=b_hid[:, 0:1]).then_inc(M["rel0"], 1)

            def outs(v, b):
                need(eng, M[f"st{b}"], (v - b) * 8)
                need(eng, M["pout"], v + 1)
                copy(view(o_sb[b], 0, [[F, J], [J * F, NQ], [1, F]]), view(p_o, 0, [[P, J], [F, NQ], [1, F]])).then_inc(M["aout"], 1)

            def front(v, b):
                reorder(v, b)
                rs(v, b)
                xs(v, b)
                next_idx(3 * NC + v, v, b, M["pin"], v * 2 + 2)
                rel(v, b)

            front(0, 0)
            front(1, 1)
            for v in (2, 3):
                outs(v - 2, v % 2)
                front(v, v % 2)
            with eng.Fori(2, NC // 2 - 1) as i:
                outs(i * 2 - 2, 0)
                front(i * 2, 0)
                outs(i * 2 - 1, 1)
                front(i * 2 + 1, 1)
            outs(NC - 4, 0)
            for v in (NC - 2, NC - 1):
                reorder(v, v % 2)
                rs(v, v % 2)
                xs(v, v % 2)
                rel(v, v % 2)
                outs(v - 1, 1 - v % 2)
            outs(NC - 1, 1)
            node(4)

        @block.vector
        def _(eng):
            v_ = nc.vector
            chain = [0]

            def link(ins, s=S["dve"]):
                chain[0] += 1
                ins.then_inc(s, 1)
                eng.wait_ge(s, chain[0])

            for b in range(2):
                v_.memset(adf[b][:, :], 0.0)
                v_.memset(mb[b][:, :], 0.0)
                v_.memset(s_b[b][:, :], 0.0)
                link(v_.memset(d_b[b][:, :], 0.0))
            eng.wait_ge(S["const"], 3)
            link(v_.tensor_scalar(nid_half[:, :], nid[:, :], -0.5, None, ALU.add))
            eng.wait_ge(S["d0"], 32)
            eng.wait_ge(S["blk"], 7)
            for q in range(NQ):
                v_.memset(same_head[0][q * F:(q + 1) * F, q * F:(q + 1) * F], 1.0)
            link(v_.tensor_copy(d0f[:, :], d0i[:, :]))
            for a in range(TU):
                last = v_.tensor_scalar(view(x1_nm, a * 112, [[1, 112]], parts=112), ident[0:112, 0:112], d0f[:, a:a + 1], None, ALU.mult)
            last.then_inc(S["pdiag"], 1)
            eng.wait_ge(S["pbc"], 2)
            v_.tensor_copy(view(x1_nm, SAMPLES, [[1, 448]]), bank[0][:, 0:448])
            link(v_.tensor_copy(view(x1_nm, SAMPLES + 448, [[1, SAMPLES - 448]]), bank[1][:, 0:SAMPLES - 448]))
            eng.sem_inc(S["samples"], 1)
            def find_row(u, b, base):
                need(eng, S["sums"], u * TU + TU)
                tick(eng, "ticks2")
                sums = sign_sum[:, u * TU:(u + 1) * TU] if isinstance(u, int) else sign_sum[:, bass.ds(u * TU, TU)]
                v_.tensor_scalar(cnt_a[:, b, :], sums, 0.5, SAMPLES / 2 - 1, ALU.mult, ALU.add).then_inc(S["tickv"], 1)
                eng.wait_ge(S["tickv"], base + 1)
                v_.tensor_scalar(cnt_a[:, b, :], cnt_a[:, b, :], 0.0, None, ALU.max).then_inc(S["tickv"], 1)
                eng.wait_ge(S["tickv"], base + 2)
                v_.tensor_scalar(rowidx[:, b, :], cnt_a[:, b, :], float(LEAD // L), None, ALU.add).then_inc(S["cnta"], 1)

            def count_b(u, b, base):
                need(eng, S[f"row{b}"], (u - b) * (TU * 8) + TU * 16)
                tick(eng, "ticks2")
                for t in range(TU):
                    at = u * TU + t
                    sc = nid[:, at:at + 1] if isinstance(at, int) else nid[:, bass.ds(at, 1)]
                    v_.tensor_scalar(view(x1_nm, 3 * SAMPLES, [[1, L]]), rowbuf[:, b, t, :], sc, None, ALU.is_lt, ALU.add,
                                     accum_out=cnt_b[:, b, t:t + 1]).then_inc(S["tickv"], 1)
                    eng.wait_ge(S["tickv"], base + t + 1)
                o = start_nm[:, u * TU:(u + 1) * TU] if isinstance(u, int) else start_nm[:, bass.ds(u * TU, TU)]
                v_.scalar_tensor_tensor(o, cnt_a[:, b, :], float(L), cnt_b[:, b, :], ALU.mult, ALU.add).then_inc(S["cntb"], 1)
                need(eng, S["cntb"], u + 1)

            def restarts(k, base):
                o, d = (t[:, k, :] if isinstance(k, int) else t[:, bass.ds(k, 1), :].rearrange("p a l -> p (a l)") for t in (rbf, dt_))
                v_.tensor_tensor(o, d[:, 1:L + 1], d[:, 0:L], ALU.is_equal).then_inc(S["tickv"], 1)
                eng.wait_ge(S["tickv"], base + 1)
                v_.tensor_scalar(o, o, 2 * BIG, -BIG, ALU.mult, ALU.add).then_inc(S["tickv"], 1)
                eng.wait_ge(S["tickv"], base + 2)

            K_S = TU + 2
            find_row(0, 0, 0)
            find_row(1, 1, 2)
            eng.wait_ge(S["src"], 16 * 8)
            v_.tensor_copy(st_[:, :, :].bitcast(fp32), st_[:, :, :]).then_inc(S["cast"], 1)
            for u in (0, 1):
                count_b(u, u, 4 + u * K_S)
                find_row(u + 2, u, 4 + u * K_S + TU)
            eng.wait_ge(S["tiles"], 16 * 8)
            for k in (0, 1):
                restarts(k, 4 + 2 * K_S + 2 * k)
            eng.wait_ge(S["const"], 4)
            eng.wait_ge(S["par"], N_PAR * 16)
            for l in range(3):
                for a in range(NQ):
                    v_.tensor_copy(w_rep[l][:, a, :], w_in[l][:, :])
                v_.tensor_scalar(w_as[l][:, :], same_head[1 if l < 2 else 0][:, :], att_col[l][:, 0:1], None, ALU.mult)
                last = v_.tensor_copy(w_att[l][:, 0:F], ident[0:F, 0:F])
            last.then_inc(S["wrep"], 1)
            for l in range(3):
                link(v_.memset(w_node[l][:, :, :], 0.0))
            before, K_I = 4 + 2 * K_S + 4, 2 * K_S + 2
            assert 2 + (NU // 2 - 2) <= 8
            with eng.Fori(2, NU // 2) as i:
                for b in range(2):
                    base = (i - 2) * K_I + (before + b * K_S)
                    count_b(i * 2 + (b - 2), b, base)
                    find_row(i * 2 + b, b, base + TU)
                restarts(i, (i - 2) * K_I + (before + 2 * K_S))
            done = before + (NU // 2 - 2) * K_I
            count_b(NU - 2, 0, done)
            count_b(NU - 1, 1, done + TU)
            eng.sem_inc(S["ready"], 1)
            eng.wait_ge(S["wpe"], 3)
            for l in range(3):
                for a in range(4):
                    link(v_.tensor_copy(w_node[l][F * a:F * (a + 1), a, :], bank[2 + l][F * a:F * (a + 1), 0:ROW]))
            eng.sem_inc(S["wnode"], 1)
            for k in range(NU // 2, 8):
                restarts(k, done + 2 * TU + 2 * (k - NU // 2))
            for q in range(NQ):
                last = v_.memset(rbf[0:1, 2 * q, 0:1], -BIG)
            last.then_inc(S["rw"], 1)
            eng.wait_ge(S["endr"], 16)
            link(v_.tensor_tensor(has_nm[:, :], end_nm[:, :], start_nm[:, :], ALU.is_gt))
            link(v_.tensor_scalar(tmp_a[:, :], nid[:, :], float(EP), None, ALU.add))
            link(v_.tensor_tensor(tmp_b[:, :], start_nm[:, :], tmp_a[:, :], ALU.subtract))
            link(v_.tensor_tensor(tmp_b[:, :], tmp_b[:, :], has_nm[:, :], ALU.mult))
            link(v_.tensor_tensor(tmp_b[:, :], tmp_b[:, :], tmp_a[:, :], ALU.add))
            link(v_.tensor_copy(scat_nm[:, :], tmp_b[:, :]))
            eng.wait_ge(S["xload"], 48)
            eng.sem_inc(S["scat"], 1)

            def per_node():
                link(v_.tensor_scalar(hasb_nm[:, :], has_nm[:, :], 2 * BIG, -BIG, ALU.mult, ALU.add))
                link(v_.tensor_scalar(tmp_a[:, :], end_nm[:, :], -1.0, 0.0, ALU.add, ALU.max))
                link(v_.tensor_copy(last_nm[:, :], tmp_a[:, :]))
                for q in range(3):
                    link(v_.tensor_scalar(tmp_a[:, :], start_nm[:, :], float((q + 1) * Q), None, ALU.is_lt))
                    link(v_.tensor_scalar(tmp_b[:, :], end_nm[:, :], float((q + 1) * Q), None, ALU.is_gt))
                    link(v_.tensor_tensor(tmp_a[:, :], tmp_a[:, :], tmp_b[:, :], ALU.mult))
                    link(v_.tensor_scalar(cross_nm[:, :, q], tmp_a[:, :], 2 * BIG, -BIG, ALU.mult, ALU.add))
                eng.wait_ge(S["act0"], 1)
                link(v_.tensor_scalar(ea_s[:, 2:3], ea_s[:, 1:2], 0.1, None, ALU.is_lt))
                link(v_.tensor_scalar(ea_s[:, 3:4], ea_s[:, 2:3], -1.0, 1.0, ALU.mult, ALU.add))
                link(v_.scalar_tensor_tensor(ea_s[:, 3:4], ea_s[:, 3:4], ea_s[:, 1:2], ea_s[:, 2:3], ALU.mult, ALU.add))

            nchain = [0]

            def node(step):
                n0 = step * NU
                K = CHAIN[step]
                base0 = nchain[0]

                def chunk(u, b):
                    base = u * K + base0
                    k = [0]

                    def lk(ins):
                        k[0] += 1
                        ins.then_inc(D["chain"], 1)
                        eng.wait_ge(D["chain"], base + k[0])

                    def part(t, w=None):
                        if w is None:
                            return t[:, u * TU:(u + 1) * TU] if isinstance(u, int) else t[:, bass.ds(u * TU, TU)]
                        return t[:, u * TU:(u + 1) * TU, :] if isinstance(u, int) else t[:, bass.ds(u * TU, TU), :]

                    n = n0 + u
                    if step:
                        need(eng, D[f"g{b}"], ((step - 1) * NU // 2) * TU * 16 + ((u - b) * (TU * 8) + TU * 16))
                        if isinstance(u, int) and u == 0:
                            eng.wait_ge(D["ends"], 16 * step)
                        tick(eng, "ticks2")
                    if step == 4:
                        need(eng, D["xn"], n)
                        tick(eng, "ticks2")
                    if step < 3:
                        need(eng, D["pt"], n - 1)
                    elif step == 3:
                        need(eng, D[f"tst{b}"], TST[step] + (u - b) * (16 if step < 3 else 8))
                        need(eng, D[f"s{b}"], (step * NU // 2) * TU * 16 + (u - b) * (TU * 8))
                        if isinstance(u, int) and u < 2:
                            need(eng, D["pt"], 3 * NU)
                        tick(eng, "ticks2")
                    if step == 0:
                        v_.tensor_copy(xn[b][:, :, :], part(x_nm, 1)).then_inc(D["xn"], 1)
                        return 0
                    G = ng[b]

                    def coef(i):
                        return view(k4, i * 2 * TU, [[2, TU], [1, 2], [0, 16]])

                    if step < 4:
                        lk(v_.tensor_copy(m4[:, 0, :, :], G[:, :, F + 2:OW]))
                        cr = part(cross_nm, 1)
                        cross_b = bass.AP(tensor=cr.tensor, offset=cr.offset, ap=[[NT * 3, P], [1, 3], [3, TU], [0, 2]])
                        lk(v_.tensor_tensor(m4[:, 1:4, :, :], cross_b, view(ends, F + 2, [[OW, 3], [0, TU], [1, 2]]), ALU.min))
                        lk(v_.tensor_reduce(nm[:, :, :].rearrange("p t h -> p (t h)"), view(m4, 0, [[1, 2 * TU], [2 * TU, 4]]), AX.X, ALU.max))
                        v_.tensor_tensor(m4[:, :, :, :].rearrange("p a t h -> p a (t h)"), m4[:, :, :, :].rearrange("p a t h -> p a (t h)"),
                                         view(nm, 0, [[0, 4], [1, 2 * TU]]), ALU.subtract).then_inc(D["dif"], 1)
                        need(eng, D["exp"], n - NU + 1)
                        v_.tensor_tensor(d4[:, 0, :, :], w4[:, 0, :, :], G[:, :, F:F + 2], ALU.mult)
                        lk(v_.tensor_tensor(d4[:, 1:4, :, :], w4[:, 1:4, :, :], view(ends, F, [[OW, 3], [0, TU], [1, 2]]), ALU.mult))
                        lk(v_.tensor_reduce(dn[:, :, :].rearrange("p t h -> p (t h)"), view(d4, 0, [[1, 2 * TU], [2 * TU, 4]]), AX.X, ALU.add))
                        lk(v_.tensor_scalar(dn[:, :, :], dn[:, :, :], 1e-16, None, ALU.add))
                        lk(v_.reciprocal(dn[:, :, :], dn[:, :, :]))
                        hs = part(has_nm)
                        lk(v_.tensor_tensor(dn[:, :, :], dn[:, :, :], bass.AP(tensor=hs.tensor, offset=hs.offset, ap=[[NT, P], [1, TU], [0, 2]]), ALU.mult))
                        lk(v_.tensor_tensor(k4[:, :, :, :].rearrange("p a t h -> p a (t h)"), w4[:, :, :, :].rearrange("p a t h -> p a (t h)"),
                                            view(dn, 0, [[0, 4], [1, 2 * TU]]), ALU.mult))
                        zz = view(z, 0, [[F, TU], [16, 2], [1, 16]])
                        zz2 = view(z2, 0, [[F, TU], [16, 2], [1, 16]])
                        lk(v_.tensor_tensor(zz, view(G, 0, [[OW, TU], [16, 2], [1, 16]]), coef(0), ALU.mult))
                        for q in range(3):
                            lk(v_.tensor_tensor(zz2, view(ends, q * OW, [[0, TU], [16, 2], [1, 16]]), coef(q + 1), ALU.mult))
                            lk(v_.tensor_tensor(z[:, :, :], z[:, :, :], z2[:, :, :], ALU.add))
                        lk(v_.tensor_tensor(z[:, :, :], z[:, :, :], view(bias[step - 1], 0, [[0, TU], [1, F]]), ALU.add))
                    if step == 1:
                        lk(v_.tensor_scalar(z[:, :, :], z[:, :, :], ea_s[:, 3:4], None, ALU.mult))
                        lk(v_.scalar_tensor_tensor(z[:, :, :], z[:, :, :], 0.05, z[:, :, :], ALU.mult, ALU.add))
                    if step in (1, 2):
                        v_.tensor_scalar(z2[:, :, :], z[:, :, :], 0.0, None, ALU.min).then_inc(D["zmin"], 1)
                        need(eng, D["zexp"], n - NU + 1)
                        lk(v_.scalar_tensor_tensor(z[:, :, :], z[:, :, :], 0.0, e_sb[:, :, :], ALU.max, ALU.add))
                        lk(v_.tensor_scalar(z[:, :, :], z[:, :, :], -1.0, 3.0, ALU.add, ALU.min))
                        v_.tensor_scalar(xn[b][:, :, :], z[:, :, :], -3.0, None, ALU.max).then_inc(D["xn"], 1)
                        return k[0]
                    if step == 4:
                        lk(v_.tensor_copy(z[:, :, :], G[:, :, 0:F]))
                        cr = part(cross_nm, 1)
                        for q in range(3):
                            lk(v_.tensor_tensor(z2[:, :, :], view(ends, q * OW, [[0, TU], [1, F]]),
                                                bass.AP(tensor=cr.tensor, offset=cr.offset + q, ap=[[NT * 3, P], [3, TU], [0, F]]), ALU.min))
                            lk(v_.tensor_tensor(z[:, :, :], z[:, :, :], z2[:, :, :], ALU.max))
                        hs = part(hasb_nm)
                        lk(v_.tensor_tensor(z[:, :, :], z[:, :, :], bass.AP(tensor=hs.tensor, offset=hs.offset, ap=[[NT, P], [1, TU], [0, F]]), ALU.min))
                        lk(v_.tensor_tensor(z[:, :, :], z[:, :, :], view(bias2, 0, [[0, TU], [1, F]]), ALU.add))
                        lk(v_.tensor_tensor(z[:, :, :], z[:, :, :], part(x1_nm, 1), ALU.max))
                    lk(v_.tensor_tensor(z[:, :, :], z[:, :, :], part(x_nm if step == 3 else x1_nm, 1), ALU.add))
                    lk(v_.tensor_reduce(row2[:, :], z[:, :, :], AX.X, ALU.add))
                    lk(v_.tensor_scalar(row2[:, :], row2[:, :], 1.0 / F, None, ALU.mult))
                    lk(v_.tensor_tensor(z[:, :, :], z[:, :, :], view(row2, 0, [[1, TU], [0, F]]), ALU.subtract))
                    lk(v_.tensor_tensor(z2[:, :, :], z[:, :, :], z[:, :, :], ALU.mult))
                    lk(v_.tensor_reduce(row1[:, :], z2[:, :, :], AX.X, ALU.add))
                    v_.tensor_scalar(row1[:, :], row1[:, :], 1.0 / F, LN_EPS, ALU.mult, ALU.add).then_inc(D["var"], 1)
                    need(eng, D["std"], (step - 3) * NU + u + 1)
                    lk(v_.reciprocal(row2[:, :], std[:, :]))
                    if step == 3:
                        lk(v_.tensor_tensor(xn[b][:, :, :], z[:, :, :], view(row2, 0, [[1, TU], [0, F]]), ALU.mult))
                        v_.tensor_copy(part(x1_nm, 1), xn[b][:, :, :]).then_inc(D["xn"], 1)
                    else:
                        v_.tensor_tensor(part(x1_nm, 1), z[:, :, :], view(row2, 0, [[1, TU], [0, F]]), ALU.mult).then_inc(D["xn"], 1)
                    return k[0]

                got = chunk(0, 0)
                assert got == K, (step, got)
                assert chunk(1, 1) == K
                with eng.Fori(1, NU // 2) as i:
                    chunk(i * 2, 0)
                    chunk(i * 2 + 1, 1)
                nchain[0] += NU * K

            for layer in range(3):
                node(layer)
                if layer == 0:
                    per_node()
                slope = 0.01 if layer == 0 else 0.2

                def chunk(v, b):
                    n = layer * NC + v
                    pin, rs, me = n * 5, n, n * 10
                    need(eng, E["rs"], rs + 1)
                    need(eng, E["pin"], pin + 3)
                    need(eng, E["dve"], me)
                    v_.tensor_tensor_scan(adf[b][:, :], r_sb[b][:, :], p_ad[:, :], adf[1 - b][:, L - 1:L], ALU.min, ALU.max).then_inc(E["dve"], 1)
                    need(eng, E["pin"], pin + 5)
                    need(eng, E["dve"], me + 1)
                    v_.tensor_tensor(u_sb[:, :], adf[b][:, :], p_as[:, :], ALU.add).then_inc(E["dve"], 1)
                    need(eng, E["dve"], me + 2)
                    v_.scalar_tensor_tensor(lm[:, 0, :], u_sb[:, :], slope, u_sb[:, :], ALU.mult, ALU.max).then_inc(E["dve"], 1)
                    need(eng, E["pout"], (n - 1) * 2)
                    v_.tensor_copy(mb[b][:, 0:1], mb[1 - b][:, L:L + 1]).then_inc(E["dve"], 1)
                    need(eng, E["dve"], me + 4)
                    v_.tensor_tensor_scan(mb[b][:, 1:L + 1], r_sb[b][:, :], lm[:, 0, :], mb[b][:, 0:1], ALU.min, ALU.max).then_inc(E["dve"], 1)
                    need(eng, E["dve"], me + 5)
                    v_.tensor_tensor(lm[:, 1, :], mb[b][:, 0:L], r_sb[b][:, :], ALU.min).then_inc(E["dve"], 1)
                    need(eng, E["dve"], me + 6)
                    need(eng, E["exp"], n)
                    v_.tensor_tensor(dif[:, :, :], lm[:, :, :], view(mb[b], 1, [[0, 2], [1, L]]), ALU.subtract).then_inc(E["dve"], 1)
                    need(eng, E["exp"], n + 1)
                    v_.tensor_tensor(ph[:, :], pc[:, 0, :], p_h[b][:, :], ALU.mult).then_inc(E["dve"], 1)
                    need(eng, E["dve"], me + 8)
                    v_.tensor_tensor_scan(s_b[b][:, :], pc[:, 1, :], ph[:, :], s_b[1 - b][:, L - 1:L], ALU.mult, ALU.add).then_inc(E["dve"], 1)
                    v_.tensor_tensor_scan(d_b[b][:, :], pc[:, 1, :], pc[:, 0, :], d_b[1 - b][:, L - 1:L], ALU.mult, ALU.add).then_inc(E["dve"], 1)
                chunk(0, 0)
                chunk(1, 1)
                with eng.Fori(1, NC // 2) as i:
                    chunk(i * 2, 0)
                    chunk(i * 2 + 1, 1)
            eng.wait_ge(E["dve"], 3 * NC * 10)
            eng.wait_ge(E["pout"], 3 * NC * 2)
            node(3)

            def mlp(v, b):
                need(eng, M["rs"], v + 1)
                need(eng, M["pin"], v * 2 + 2)
                need(eng, M["scan"], v)
                need(eng, M["phid"], v * 2)
                v_.tensor_copy(xe_t, p_xe[:, :]).then_inc(M["xe"], 1)
                v_.tensor_tensor_scan(adf[b][:, :], r_sb[b][:, :], p_xd[:, :], adf[1 - b][:, L - 1:L], ALU.min, ALU.max).then_inc(M["fill"], 1)
                need(eng, M["phid"], v * 2 + 2)
                v_.tensor_scalar(hid[1][:, :], p_hid[1][:, :], b_hid[:, 0:1], 0.0, ALU.add, ALU.max).then_inc(M["rel1"], 1)
                need(eng, M["pv"], v + 1)
                need(eng, M["pout"], v - 1)
                v_.tensor_tensor_scan(s_b[b][:, :], r_sb[b][:, :], p_v[:, :], s_b[1 - b][:, L - 1:L], ALU.min, ALU.max).then_inc(M["scan"], 1)
            mlp(0, 0)
            mlp(1, 1)
            with eng.Fori(1, NC // 2) as i:
                mlp(i * 2, 0)
                mlp(i * 2 + 1, 1)
            node(4)


_INS = ["x", "src", "dst", "edge_attr_32"] + [f"L0_gnn_{n}{l}" for l in (1, 2, 3) for n in ("W", "att_s", "att_d", "b")] \
    + ["L0_gnn_ea1", "L1_gnn_W1", "L1_gnn_b1", "L1_gnn_W2", "L1_gnn_b2"]


def kernel(**inputs):
    import numpy as np
    import concourse.bacc as _bacc
    from concourse import mybir as _mybir
    from concourse.bass_utils import run_bass_kernel_spmd as _run

    nc = _bacc.Bacc("TRN2", target_bir_lowering=False, num_devices=1)
    arrays, aps = {}, {}
    for name in _INS:
        a = np.ascontiguousarray(inputs[name])
        arrays["in_" + name] = a
        aps[name] = nc.dram_tensor("in_" + name, a.shape, _mybir.dt.from_np(a.dtype), kind="ExternalInput").ap()
    out = nc.dram_tensor("out_0", (N_NODES, F), _mybir.dt.float32, kind="ExternalOutput").ap()
    build(nc, aps, out)
    r = _run(nc, [arrays], core_ids=[0])
    return r.results[0]["out_0"]
```
